# Optimizing a Trainium2 kernel written in Bass

```python
import numpy as np
import jax
import jax.numpy as jnp

def _softmax(x, axis=-1):
    return jax.nn.softmax(x, axis=axis)

def _gelu(x):
    return jax.nn.gelu(x, approximate=True)

def _silu(x):
    return jax.nn.silu(x)

def _sigmoid(x):
    return jax.nn.sigmoid(x)

def _layernorm(x, axis=-1, eps=1e-05):
    m = jnp.mean(x, axis=axis, keepdims=True)
    v = jnp.var(x, axis=axis, keepdims=True)
    return (x - m) / jnp.sqrt(v + eps)

def _scatter_add(tgt, idx, src, axis=0):
    return tgt.at[idx].add(src)

def _segment_sum(src, seg, n):
    return jax.ops.segment_sum(src, seg, n)
kernel_name = 'mk_cond_resid_d1_seqx_r4_8652c8'

def setup_inputs(seed: int=0):
    np.random.seed(seed)
    _w = jnp.asarray

    def _rec_inputs():
        import jax
        import jax.numpy as jnp
        _rk = jax.random.key(seed)
        x = 0.0001044 + 1 * jax.random.normal(jax.random.fold_in(_rk, 1), (32, 256, 256), jnp.float32)
        _lenS = 256 - jax.random.randint(jax.random.fold_in(_rk, 7), (32,), 0, max(1, 256 // 4) + 1, jnp.int32)
        _lenS2 = 256 - jax.random.randint(jax.random.fold_in(_rk, 8), (32,), 0, max(1, 256 // 4) + 1, jnp.int32)
        cond_1024 = 0.00141218 + 0.997886 * jax.random.normal(jax.random.fold_in(_rk, 11), (32, 256), jnp.float32)
        return (x, cond_1024)
    x, cond_1024 = _rec_inputs()

    def _L0_cond_setup():
        import jax, jax.numpy as jnp
        import numpy as np
        B, T, C = (64, 128, 256)
        key = jax.random.key(seed)
        ks = jax.random.split(key, 17)
        s_in = 1.0 / np.sqrt(C)

        def lin(kw, kb, fan_in):
            s = 1.0 / np.sqrt(fan_in)
            W = jax.random.uniform(kw, (C, fan_in), jnp.float32, -s, s)
            b = jax.random.uniform(kb, (C,), jnp.float32, -s, s)
            return (W, b)
        Wxz, bxz = lin(ks[0], ks[1], C)
        Whz, bhz = lin(ks[2], ks[3], C)
        Wxr, bxr = lin(ks[4], ks[5], C)
        Whr, bhr = lin(ks[6], ks[7], C)
        Wxh, bxh = lin(ks[8], ks[9], C)
        Whh, bhh = lin(ks[10], ks[11], C)
        Whq, bhq = lin(ks[12], ks[13], C)
        X = jax.random.normal(ks[14], (B, T, C), jnp.float32)
        h0 = jax.random.normal(ks[15], (B, C), jnp.float32)
        return {'X': X, 'h0': h0, 'Wxz': Wxz, 'bxz': bxz, 'Whz': Whz, 'bhz': bhz, 'Wxr': Wxr, 'bxr': bxr, 'Whr': Whr, 'bhr': bhr, 'Wxh': Wxh, 'bxh': bxh, 'Whh': Whh, 'bhh': bhh, 'Whq': Whq, 'bhq': bhq}
    _L0_cond_all = _L0_cond_setup()
    _L0_cond_in = {k: v for k, v in _L0_cond_all.items() if k in ('Wxz', 'bxz', 'Whz', 'bhz', 'Wxr', 'bxr', 'Whr', 'bhr', 'Wxh', 'bxh', 'Whh', 'bhh', 'Whq', 'bhq')}
    del _L0_cond_all
    return {'x': x, 'cond_1024': cond_1024, 'L0_cond_Wxz': _L0_cond_in['Wxz'], 'L0_cond_bxz': _L0_cond_in['bxz'], 'L0_cond_Whz': _L0_cond_in['Whz'], 'L0_cond_bhz': _L0_cond_in['bhz'], 'L0_cond_Wxr': _L0_cond_in['Wxr'], 'L0_cond_bxr': _L0_cond_in['bxr'], 'L0_cond_Whr': _L0_cond_in['Whr'], 'L0_cond_bhr': _L0_cond_in['bhr'], 'L0_cond_Wxh': _L0_cond_in['Wxh'], 'L0_cond_bxh': _L0_cond_in['bxh'], 'L0_cond_Whh': _L0_cond_in['Whh'], 'L0_cond_bhh': _L0_cond_in['bhh'], 'L0_cond_Whq': _L0_cond_in['Whq'], 'L0_cond_bhq': _L0_cond_in['bhq']}

def reference(x, cond_1024, L0_cond_Wxz, L0_cond_bxz, L0_cond_Whz, L0_cond_bhz, L0_cond_Wxr, L0_cond_bxr, L0_cond_Whr, L0_cond_bhr, L0_cond_Wxh, L0_cond_bxh, L0_cond_Whh, L0_cond_bhh, L0_cond_Whq, L0_cond_bhq):
    import jax
    import jax.numpy as jnp

    def _L0_cond_ref(X, h0, Wxz, bxz, Whz, bhz, Wxr, bxr, Whr, bhr, Wxh, bxh, Whh, bhh, Whq, bhq):
        import jax, jax.numpy as jnp
        import numpy as np
        B, T, C = (64, 128, 256)
        Xz = jnp.einsum('btc,hc->tbh', X, Wxz) + bxz
        Xr = jnp.einsum('btc,hc->tbh', X, Wxr) + bxr
        Xh = jnp.einsum('btc,hc->tbh', X, Wxh) + bxh

        def step(H, xs):
            xz, xr, xh = xs
            Z = jax.nn.sigmoid(xz + H @ Whz.T + bhz)
            R = jax.nn.sigmoid(xr + H @ Whr.T + bhr)
            H_tilda = jnp.tanh(xh + R * H @ Whh.T + bhh)
            H_new = Z * H + (1.0 - Z) * H_tilda
            Y = H_new @ Whq.T + bhq
            return (H_new, Y)
        _, Ys = jax.lax.scan(step, h0, (Xz, Xr, Xh))
        return jnp.transpose(Ys, (1, 0, 2))
    x = x + _L0_cond_ref(x, cond_1024, L0_cond_Wxz, L0_cond_bxz, L0_cond_Whz, L0_cond_bhz, L0_cond_Wxr, L0_cond_bxr, L0_cond_Whr, L0_cond_bhr, L0_cond_Wxh, L0_cond_bxh, L0_cond_Whh, L0_cond_bhh, L0_cond_Whq, L0_cond_bhq)
    return x

_drawn_inputs = setup_inputs


def setup_inputs(seed=0):
    import zlib

    import numpy as np

    out = dict(_drawn_inputs(seed))
    spreads = {}
    factors = {'L0_cond_bxz': 21.65,
     'L0_cond_Whz': 3.845,
     'L0_cond_bhz': 23.279,
     'L0_cond_Wxr': 8.0,
     'L0_cond_bxr': 64.0,
     'L0_cond_Whr': 40.972,
     'L0_cond_bhr': 64.0,
     'L0_cond_bxh': 3.155,
     'L0_cond_bhh': 3.53}
    for name, (base, spread) in spreads.items():
        noise = np.random.default_rng([zlib.crc32(name.encode()), seed]).standard_normal(out[name].shape)
        drawn = base * np.exp(spread * noise) if base else spread * noise
        out[name] = jnp.asarray(drawn.astype(out[name].dtype))
    for name, factor in factors.items():
        out[name] = (out[name] * factor).astype(out[name].dtype)
    return out
```

```python
import concourse.bass as bass
from concourse import mybir
from contextlib import ExitStack

B = 32
T = 256
C = 256
P = 128
K = C // P
NQ = P // B
RW = C // NQ
GS = P // B
NG = T // GS
UG = 2
US = UG * GS
NIT = NG // UG
DMA = 16
PARTS = 3
BK = 32 * PARTS
ZH_COLS = slice(0, 2 * RW)
R_COLS = slice(2 * RW, 2 * RW + C)
Q_COLS = slice(2 * RW + C, 2 * RW + 2 * C)
BCOLS = 2 * RW + 2 * C


def gru_kernel(nc, xt, xrows, h0t, wxr, wxz, wxh, whr, whz, whh, whq, bzh, br, bq, sel, out):
    fp32 = mybir.dt.float32
    bf16 = mybir.dt.bfloat16
    ALU = mybir.AluOpType
    ACT = mybir.ActivationFunctionType

    ctx = ExitStack()
    with ctx:
        def sb(name, shape, dt=fp32):
            return ctx.enter_context(nc.sbuf_tensor(name, shape, dt))

        def pb(name, shape):
            return ctx.enter_context(nc.psum_tensor(name, shape, fp32))

        def sem(name):
            return ctx.enter_context(nc.semaphore(name))

        wxr_sb = sb("wxr_sb", [P, K, K, P])
        whr_sb = sb("whr_sb", [P, K, K, P])
        wxzh_sb = sb("wxzh_sb", [P, K, NQ, 2, RW])
        whz_sb = sb("whz_sb", [P, K, NQ, RW])
        whh_sb = sb("whh_sb", [P, K, NQ, RW])
        whq_sb = sb("whq_sb", [P, K, C])
        b_raw = sb("b_raw", [2 * NQ, BCOLS])
        b_rest = sb("b_rest", [2 * NQ, PARTS - 1, BCOLS])
        b_low = sb("b_low", [2 * NQ, PARTS, BCOLS], bf16)
        b_parts = sb("b_parts", [BK, BCOLS], bf16)
        sel_raw = sb("sel_raw", [BK, P])
        sel_sb = sb("sel_sb", [BK, P], bf16)
        ones_sb = sb("ones_sb", [BK, P], bf16)
        xr_sb = sb("xr_sb", [P, UG, K, P])
        xz_sb = sb("xz_sb", [P, UG, K, P])
        xrow_sb = sb("xrow_sb", [P, UG, C])
        orow_sb = sb("orow_sb", [P, UG, C])
        h_sb = sb("h_sb", [P, K, US, B])
        r_sb = sb("r_sb", [P, K, B])
        rh_sb = sb("rh_sb", [P, K, B])
        z_sb = sb("z_sb", [P, RW])
        zt_sb = sb("zt_sb", [P, K, B])
        zh_sb = sb("zh_sb", [P, K, B])
        c_sb = sb("c_sb", [P, RW])
        u_sb = sb("u_sb", [P, RW])
        ut_sb = sb("ut_sb", [P, K, B])

        r_ps = [[pb(f"r_ps{p}{o}", [P, 512]) for o in range(K)] for p in range(UG)]
        zh_ps = [pb(f"zh_ps{p}", [P, 512]) for p in range(2)]
        y_ps = [pb(f"y_ps{p}", [P, 512]) for p in range(UG)]

        s_wr = sem("s_wr")
        s_wz = sem("s_wz")
        s_b = sem("s_b")
        s_init = sem("s_init")
        s_xr = [sem(f"s_xr{p}") for p in range(UG)]
        s_xz = [sem(f"s_xz{p}") for p in range(UG)]
        s_xrow = [sem(f"s_xrow{p}") for p in range(UG)]
        s_out = [sem(f"s_out{p}") for p in range(UG)]
        s_zero = sem("s_zero")
        s_split = sem("s_split")
        s_bias = sem("s_bias")
        s_xr_used = sem("s_xr_used")
        s_xz_used = sem("s_xz_used")
        s_r_ps = [sem(f"s_r_ps{o}") for o in range(K)]
        s_z_ps = sem("s_z_ps")
        s_c_ps = sem("s_c_ps")
        s_y_ps = sem("s_y_ps")
        s_r = [sem(f"s_r{o}") for o in range(K)]
        s_z = sem("s_z")
        s_c = sem("s_c")
        s_rh = [sem(f"s_rh{k}") for k in range(K)]
        s_zt = sem("s_zt")
        s_zh = sem("s_zh")
        s_u = [sem(f"s_u{k}") for k in range(K)]
        s_ut = [sem(f"s_ut{k}") for k in range(K)]
        s_h = [sem(f"s_h{k}") for k in range(K)]
        s_y = sem("s_y")

        block = ctx.enter_context(nc.Block())

        def iterations(eng, body):
            body(0, True, False)
            with eng.Fori(1, NIT - 1) as i:
                body(i, False, False)
            body(NIT - 1, False, True)

        @block.sync
        def _(sp):
            sp.dma_start(wxr_sb[:], wxr).then_inc(s_wr, DMA)
            sp.dma_start(xr_sb[:, 0], xt[0]).then_inc(s_xr[0], DMA)
            sp.dma_start(xz_sb[:, 0], xt[0]).then_inc(s_xz[0], DMA)
            sp.dma_start(wxzh_sb[:, :, :, 0], wxz).then_inc(s_wz, DMA)
            sp.dma_start(wxzh_sb[:, :, :, 1], wxh).then_inc(s_wz, DMA)
            sp.dma_start(whz_sb[:], whz).then_inc(s_wz, DMA)
            sp.dma_start(whh_sb[:], whh).then_inc(s_wz, DMA)
            sp.dma_start(xr_sb[:, 1], xt[1]).then_inc(s_xr[1], DMA)
            sp.dma_start(xz_sb[:, 1], xt[1]).then_inc(s_xz[1], DMA)
            sp.dma_start(whq_sb[:], whq).then_inc(s_wz, DMA)
            for p in range(UG):
                sp.dma_start(xrow_sb[:, p], xrows[p]).then_inc(s_xrow[p], DMA)

            def body(i, first, last):
                for p in range(UG):
                    g = i * UG + p
                    if not first:
                        sp.wait_ge(s_y, g - 1)
                        sp.dma_start(out[g - 2], orow_sb[:, p]).then_inc(s_out[p], DMA)
                        sp.dma_start(xrow_sb[:, p], xrows[g]).then_inc(s_xrow[p], DMA)
                    if not last:
                        sp.wait_ge(s_xz_used, g + 1)
                        sp.dma_start(xz_sb[:, p], xt[g + 2]).then_inc(s_xz[p], DMA)
                    if not last:
                        sp.wait_ge(s_xr_used, g + 1)
                        sp.dma_start(xr_sb[:, p], xt[g + 2]).then_inc(s_xr[p], DMA)

            iterations(sp, body)
            for p in range(UG):
                g = NG - UG + p
                sp.wait_ge(s_y, g + 1)
                sp.dma_start(out[g], orow_sb[:, p]).then_inc(s_out[p], DMA)
            for p in range(UG):
                sp.wait_ge(s_out[p], DMA * NIT)

        @block.scalar
        def _(act):
            act.dma_start(sel_raw[:], sel).then_inc(s_b, DMA)
            act.wait_ge(s_zero, 1)
            act.dma_start(b_raw[:, ZH_COLS], bzh).then_inc(s_b, DMA)
            act.dma_start(b_raw[0:2, R_COLS], br).then_inc(s_b, DMA)
            act.dma_start(b_raw[0:1, Q_COLS], bq).then_inc(s_b, DMA)
            act.dma_start(h_sb[:, :, US - 1], h0t).then_inc(s_init, DMA)
            act.dma_start(whr_sb[:], whr).then_inc(s_wr, DMA)

            def body(i, first, last):
                for u in range(US):
                    t = i * US + u
                    cols = slice(B * (u % GS), B * (u % GS) + B)
                    for o in range(K):
                        act.wait_ge(s_r_ps[o], t + 1)
                        nc.scalar.activation(r_sb[:, o], r_ps[u // GS][o][:, cols],
                                             ACT.Sigmoid).then_inc(s_r[o], 1)
                    act.wait_ge(s_z_ps, t + 1)
                    nc.scalar.activation(z_sb[:], zh_ps[u % 2][:, 0:RW], ACT.Sigmoid).then_inc(s_z, 1)
                    act.wait_ge(s_c_ps, t + 1)
                    nc.scalar.activation(c_sb[:], zh_ps[u % 2][:, RW:2 * RW], ACT.Tanh).then_inc(s_c, 1)

            iterations(act, body)

        @block.vector
        def _(dve):
            nc.vector.memset(b_raw[:], 0.0).then_inc(s_zero, 1)
            nc.vector.memset(b_parts[:], 0.0).then_inc(s_zero, 1)
            nc.vector.memset(ones_sb[:], 1.0).then_inc(s_bias, 1)
            dve.wait_ge(s_b, 4 * DMA)
            dve.wait_ge(s_zero, 2)
            nc.vector.tensor_copy(sel_sb[:], sel_raw[:]).then_inc(s_bias, 1)
            rest = b_raw[:]
            for q in range(PARTS):
                nc.vector.tensor_copy(b_low[:, q], rest).then_inc(s_split, 1)
                nc.vector.tensor_copy(b_parts[32 * q:32 * q + 2 * NQ, :], rest).then_inc(s_bias, 1)
                if q < PARTS - 1:
                    dve.wait_ge(s_split, 2 * q + 1)
                    nc.vector.tensor_tensor(b_rest[:, q], rest, b_low[:, q],
                                            ALU.subtract).then_inc(s_split, 1)
                    dve.wait_ge(s_split, 2 * q + 2)
                    rest = b_rest[:, q]

            def add_rows(p):
                return nc.vector.tensor_tensor(orow_sb[:, p], y_ps[p][:, 0:C], xrow_sb[:, p], ALU.add)

            dve.wait_ge(s_init, DMA)

            def body(i, first, last):
                for u in range(US):
                    t = i * US + u
                    p = u // GS
                    g = i * UG + p
                    old = h_sb[:, :, (u - 1) % US]
                    new = h_sb[:, :, u]
                    for k in range(K):
                        dve.wait_ge(s_r[k], t + 1)
                        nc.vector.tensor_tensor(rh_sb[:, k], r_sb[:, k], old[:, k],
                                                ALU.mult).then_inc(s_rh[k], 1)
                    dve.wait_ge(s_z, t + 1)
                    nc.vector.transpose(zt_sb[:].rearrange("p k b -> p (k b)"), z_sb[:]).then_inc(s_zt, 1)
                    dve.wait_ge(s_zt, t + 1)
                    nc.vector.tensor_tensor(zh_sb[:], zt_sb[:], old, ALU.mult).then_inc(s_zh, 1)
                    if u % GS == 0 and not first:
                        dve.wait_ge(s_y_ps, g - 1)
                        dve.wait_ge(s_xrow[p], DMA * i)
                        dve.wait_ge(s_out[p], DMA * i - DMA)
                        add_rows(p).then_inc(s_y, 1)
                    dve.wait_ge(s_c, t + 1)
                    for k in range(K):
                        n = slice(B * k, B * k + B)
                        nc.vector.scalar_tensor_tensor(u_sb[:, n], z_sb[:, n], 1.0, c_sb[:, n],
                                                       ALU.subtract, ALU.mult,
                                                       reverse0=True).then_inc(s_u[k], 1)
                    for k in range(K):
                        dve.wait_ge(s_u[k], t + 1)
                        nc.vector.transpose(ut_sb[:, k], u_sb[:, B * k:B * k + B]).then_inc(s_ut[k], 1)
                    dve.wait_ge(s_zh, t + 1)
                    for k in range(K):
                        dve.wait_ge(s_ut[k], t + 1)
                        nc.vector.tensor_tensor(new[:, k], zh_sb[:, k], ut_sb[:, k],
                                                ALU.add).then_inc(s_h[k], 1)

            iterations(dve, body)
            for p in range(UG):
                g = NG - UG + p
                dve.wait_ge(s_y_ps, g + 1)
                dve.wait_ge(s_xrow[p], DMA * NIT)
                dve.wait_ge(s_out[p], DMA * (NIT - 1))
                add_rows(p).then_inc(s_y, 1)

        @block.tensor
        def _(pe):
            mm = nc.tensor.matmul

            def tiles(ps, cols, lhs, rhs, k):
                for j in range(NQ):
                    last = mm(ps[B * j:B * j + B, cols], lhs, rhs(k, j), start=False, stop=False,
                              tile_position=(0, B * j), skip_group_check=True)
                return last

            def x_part_zc(step, p):
                ps = zh_ps[step % 2]
                mm(ps[:, ZH_COLS], sel_sb[:], b_parts[:, ZH_COLS], start=True, stop=False,
                   skip_group_check=True)
                cols = slice(B * (step % GS), B * (step % GS) + B)
                for k in range(K):
                    last = tiles(ps, ZH_COLS, xz_sb[:, p, k, cols],
                                 lambda k, j: wxzh_sb[:, k, j].rearrange("p g n -> p (g n)"), k)
                if step % GS == GS - 1:
                    last.then_inc(s_xz_used, 1)

            def x_part_r(p, piece):
                o, k = divmod(piece, K)
                ps = r_ps[p][o]
                if k == 0:
                    mm(ps[:, 0:P], b_parts[:, R_COLS][:, P * o:P * o + P], ones_sb[:], start=True,
                       stop=False, skip_group_check=True)
                last = mm(ps[:, 0:P], wxr_sb[:, k, o], xr_sb[:, p, k], start=False, stop=False,
                          skip_group_check=True)
                if piece == 2 * K - 1:
                    last.then_inc(s_xr_used, 1)

            def output_part(p, piece):
                half, k = divmod(piece, K)
                n = slice(P * half, P * half + P)
                if piece == 0:
                    mm(y_ps[p][:, 0:C], ones_sb[:], b_parts[:, Q_COLS], start=True, stop=False,
                       skip_group_check=True)
                last = mm(y_ps[p][:, n], h_sb[:, k, GS * p:GS * p + GS], whq_sb[:, k, n],
                          start=False, stop=False, skip_group_check=True)
                if piece == 2 * K - 1:
                    last.then_inc(s_y_ps, 1)

            pe.wait_ge(s_bias, 2 + PARTS)
            pe.wait_ge(s_wr, 2 * DMA)
            pe.wait_ge(s_xr[0], DMA)
            for piece in range(2 * K):
                x_part_r(0, piece)
            pe.wait_ge(s_wz, 5 * DMA)
            pe.wait_ge(s_xz[0], DMA)
            x_part_zc(0, 0)
            pe.wait_ge(s_init, DMA)

            def body(i, first, last):
                for u in range(US):
                    t = i * US + u
                    p = u // GS
                    s = u % GS
                    g = i * UG + p
                    more = not (last and u == US - 1)
                    cols = slice(B * s, B * s + B)
                    old = h_sb[:, :, (u - 1) % US]
                    for k in range(K):
                        if not (first and u == 0):
                            pe.wait_ge(s_h[k], t)
                        for o in range(K):
                            for j in range(NQ):
                                q = slice(B * j, B * j + B)
                                r_mm = mm(r_ps[p][o][q, cols], whr_sb[:, k, o, q], old[:, k],
                                          start=False, stop=False, tile_position=(0, B * j),
                                          skip_group_check=True)
                            if k == K - 1:
                                r_mm.then_inc(s_r_ps[o], 1)
                    for k in range(K):
                        z_mm = tiles(zh_ps[u % 2], slice(0, RW), old[:, k],
                                     lambda k, j: whz_sb[:, k, j], k)
                    z_mm.then_inc(s_z_ps, 1)
                    if not (first and p == 0):
                        output_part(1 - p, s)
                    pe.wait_ge(s_z, t + 1)
                    for k in range(K):
                        pe.wait_ge(s_rh[k], t + 1)
                        c_mm = tiles(zh_ps[u % 2], slice(RW, 2 * RW), rh_sb[:, k],
                                     lambda k, j: whh_sb[:, k, j], k)
                    c_mm.then_inc(s_c_ps, 1)
                    if more:
                        if s == GS - 1:
                            pe.wait_ge(s_xz[1 - p], DMA * (i + 1 + p))
                        x_part_zc((u + 1) % US, (u + 1) % US // GS)
                    if not (last and p == 1):
                        if s == 0:
                            pe.wait_ge(s_xr[1 - p], DMA * (i + 1 + p))
                        x_part_r(1 - p, s)

            iterations(pe, body)
            for k in range(K):
                pe.wait_ge(s_h[k], T)
            for piece in range(2 * K):
                output_part(1, piece)


def kernel(x, cond_1024, L0_cond_Wxz, L0_cond_bxz, L0_cond_Whz, L0_cond_bhz, L0_cond_Wxr, L0_cond_bxr,
           L0_cond_Whr, L0_cond_bhr, L0_cond_Wxh, L0_cond_bxh, L0_cond_Whh, L0_cond_bhh, L0_cond_Whq,
           L0_cond_bhq):
    import numpy as np
    import concourse.bacc as bacc
    from concourse.bass_utils import run_bass_kernel_spmd

    def state_rows(w):
        w = np.asarray(w)
        return w.T.reshape(NQ, K, B, C).transpose(0, 2, 1, 3).reshape(P, K, C)

    def x_rows_of(w):
        w = np.asarray(w)
        return w.T.reshape(K, P, C).transpose(1, 0, 2)

    def by_quadrant(w):
        return w.reshape(P, K, NQ, RW)

    def by_chunk(w):
        return w.reshape(P, K, NQ, K, B).transpose(0, 1, 3, 2, 4).reshape(P, K, K, P)

    def chunked_bias(b):
        return np.asarray(b).reshape(NQ, K, B).transpose(1, 0, 2).reshape(C)

    def quadrant_bias(bz, bh):
        return np.concatenate([np.asarray(bz).reshape(NQ, RW), np.asarray(bh).reshape(NQ, RW)], axis=1)

    x = np.asarray(x)
    sel = np.zeros((BK, P), np.float32)
    for q in range(PARTS):
        for s in range(2):
            for j in range(NQ):
                sel[32 * q + NQ * s + j, B * j:B * j + B] = 1.0
    arrays = {
        "xt": x.transpose(2, 1, 0).reshape(K, P, NG, P).transpose(2, 1, 0, 3),
        "xrows": x.reshape(B, NG, GS, C).transpose(1, 2, 0, 3).reshape(NG, P, C),
        "h0t": np.asarray(cond_1024).T.reshape(NQ, K, B, B).transpose(0, 2, 1, 3).reshape(P, K, B),
        "wxr": by_chunk(x_rows_of(L0_cond_Wxr)),
        "wxz": by_quadrant(x_rows_of(L0_cond_Wxz)),
        "wxh": by_quadrant(x_rows_of(L0_cond_Wxh)),
        "whr": by_chunk(state_rows(L0_cond_Whr)),
        "whz": by_quadrant(state_rows(L0_cond_Whz)),
        "whh": by_quadrant(state_rows(L0_cond_Whh)),
        "whq": state_rows(L0_cond_Whq),
        "bzh": np.concatenate([quadrant_bias(L0_cond_bxz, L0_cond_bxh),
                               quadrant_bias(L0_cond_bhz, L0_cond_bhh)], axis=0),
        "br": np.stack([chunked_bias(L0_cond_bxr), chunked_bias(L0_cond_bhr)]),
        "bq": np.asarray(L0_cond_bhq).reshape(1, C),
        "sel": sel,
    }
    nc = bacc.Bacc("TRN2", target_bir_lowering=False, num_devices=1)
    args, feed = [], {}
    for name, a in arrays.items():
        a = np.ascontiguousarray(a)
        feed[f"in_{name}_dram"] = a
        args.append(nc.dram_tensor(f"in_{name}_dram", a.shape, mybir.dt.from_np(a.dtype),
                                   kind="ExternalInput").ap())
    args.append(nc.dram_tensor("out_dram", (NG, P, C), mybir.dt.float32, kind="ExternalOutput").ap())
    gru_kernel(nc, *args)
    r = run_bass_kernel_spmd(nc, [feed], core_ids=[0])
    rows = r.results[0]["out_dram"]
    return rows.reshape(NG, GS, B, C).transpose(2, 0, 1, 3).reshape(B, T, C)
```

```python
import concourse.bass as bass
from concourse import mybir
from contextlib import ExitStack

B = 32
T = 256
C = 256
P = 128
K = C // P
NQ = P // B
GS = P // B
NG = T // GS
UG = 2
US = UG * GS
NIT = NG // UG
DMA = 16
Z, R, N = range(3)
PARTS = 3
BR = 4
BK = 32 * PARTS
WARM = 140


def gru_kernel(nc, xt, xrows, h0t, wx, whz, whr, whh, whq, bias, bq, halves, out):
    fp32 = mybir.dt.float32
    bf16 = mybir.dt.bfloat16
    ALU = mybir.AluOpType
    ACT = mybir.ActivationFunctionType

    ctx = ExitStack()
    with ctx:
        def sb(name, shape, dt=fp32):
            return ctx.enter_context(nc.sbuf_tensor(name, shape, dt))

        def pb(name):
            return ctx.enter_context(nc.psum_tensor(name, [P, 2 * P * K], fp32))

        def sem(name):
            return ctx.enter_context(nc.semaphore(name))

        wx_sb = sb("wx_sb", [P, 3, K, C])
        whz_sb = sb("whz_sb", [P, K, C])
        whr_sb = sb("whr_sb", [P, K, C])
        whh_sb = sb("whh_sb", [P, K, C])
        whq_sb = sb("whq_sb", [P, K, C])
        b_raw = sb("b_raw", [BR, 3, P])
        b_rest = sb("b_rest", [BR, PARTS - 1, 3, P])
        b_low = sb("b_low", [BR, PARTS, 3, P], bf16)
        b_parts = sb("b_parts", [BK, 3, P], bf16)
        halves_raw = sb("halves_raw", [BK, 2, P])
        halves_sb = sb("halves_sb", [BK, 2, P], bf16)
        bq_sb = sb("bq_sb", [P, C])
        ones_sb = sb("ones_sb", [P, P], bf16)
        xt_sb = sb("xt_sb", [P, UG, K, P])
        xrow_sb = sb("xrow_sb", [P, UG, C])
        orow_sb = sb("orow_sb", [P, UG, C])
        h_sb = sb("h_sb", [P, K, US, B])
        r_sb = sb("r_sb", [P, K, B])
        rh_sb = sb("rh_sb", [P, K, B])
        z_sb = sb("z_sb", [P, K, B])
        zh_sb = sb("zh_sb", [P, K, B])
        c_sb = sb("c_sb", [P, K, B])
        u_sb = sb("u_sb", [P, K, B])

        rc_ps = [[pb(f"rc_ps{p}{o}") for o in range(K)] for p in range(UG)]
        z_ps = [pb(f"z_ps{p}") for p in range(UG)]
        y_ps = pb("y_ps")

        s_wx = sem("s_wx")
        s_wh = sem("s_wh")
        s_b = sem("s_b")
        s_bq = sem("s_bq")
        s_init = sem("s_init")
        s_xt = [sem(f"s_xt{p}") for p in range(UG)]
        s_rows = [sem(f"s_rows{p}") for p in range(UG)]
        s_zero = sem("s_zero")
        s_ones = sem("s_ones")
        s_split = sem("s_split")
        s_bias = sem("s_bias")
        s_xt_used = sem("s_xt_used")
        s_r_ps = [sem(f"s_r_ps{o}") for o in range(K)]
        s_z_ps = sem("s_z_ps")
        s_c_ps = [sem(f"s_c_ps{o}") for o in range(K)]
        s_y_ps = sem("s_y_ps")
        s_r = [sem(f"s_r{o}") for o in range(K)]
        s_z = sem("s_z")
        s_c = [sem(f"s_c{o}") for o in range(K)]
        s_rh = [sem(f"s_rh{k}") for k in range(K)]
        s_u = [sem(f"s_u{k}") for k in range(K)]
        s_h = [sem(f"s_h{k}") for k in range(K)]
        s_xb = sem("s_xb")
        s_y = sem("s_y")

        block = ctx.enter_context(nc.Block())

        def iterations(eng, body):
            body(0, True, False)
            with eng.Fori(1, NIT - 1) as i:
                body(i, False, False)
            body(NIT - 1, False, True)

        @block.sync
        def _(sp):
            sp.dma_start(halves_raw[:], halves).then_inc(s_b, DMA)
            sp.dma_start(xt_sb[:, 0], xt[0]).then_inc(s_xt[0], DMA)
            for gate in (R, N, Z):
                sp.dma_start(wx_sb[:, gate], wx[gate]).then_inc(s_wx, DMA)
            sp.dma_start(whh_sb[:], whh).then_inc(s_wh, DMA)
            sp.dma_start(whq_sb[:], whq).then_inc(s_wh, DMA)
            for p in range(UG):
                sp.dma_start(xrow_sb[:, p], xrows[p]).then_inc(s_rows[p], DMA)

            def body(i, first, last):
                for p in range(UG):
                    g = i * UG + p
                    if not last:
                        sp.wait_ge(s_xt_used, g + 1)
                        sp.dma_start(xt_sb[:, p], xt[g + 2]).then_inc(s_xt[p], DMA)
                    if not (first and p == 0):
                        sp.wait_ge(s_y, g)
                        sp.dma_start(out[g - 1], orow_sb[:, 1 - p]).then_inc(s_rows[1 - p], DMA)
                        if not (last and p == 1):
                            sp.dma_start(xrow_sb[:, 1 - p], xrows[g + 1]).then_inc(s_rows[1 - p], DMA)

            iterations(sp, body)
            sp.wait_ge(s_y, NG)
            sp.dma_start(out[NG - 1], orow_sb[:, 1]).then_inc(s_rows[1], DMA)
            for p in range(UG):
                sp.wait_ge(s_rows[p], DMA * 2 * NIT)

        @block.scalar
        def _(act):
            act.dma_start(b_raw[:], bias).then_inc(s_b, DMA)
            act.dma_start(h_sb[:, :, US - 1], h0t).then_inc(s_init, DMA)
            act.dma_start(whr_sb[:], whr).then_inc(s_wh, DMA)
            act.dma_start(whz_sb[:], whz).then_inc(s_wh, DMA)
            act.dma_start(xt_sb[:, 1], xt[1]).then_inc(s_xt[1], DMA)
            act.dma_start(bq_sb[:], bq).then_inc(s_bq, DMA)

            def body(i, first, last):
                for u in range(US):
                    t = i * US + u
                    p, s = divmod(u, GS)
                    cols = slice(B * s, B * s + B)
                    for o in range(K):
                        act.wait_ge(s_r_ps[o], t + 1)
                        nc.scalar.activation(r_sb[:, o], rc_ps[p][o][:, B * s:B * s + B],
                                             ACT.Sigmoid).then_inc(s_r[o], 1)
                    act.wait_ge(s_z_ps, t + 1)
                    z_in = z_ps[p][:, 0:K * P].rearrange("p (o c) -> p o c", o=K)[:, :, cols]
                    nc.scalar.activation(z_sb[:], z_in, ACT.Sigmoid).then_inc(s_z, 1)
                    for o in range(K):
                        act.wait_ge(s_c_ps[o], t + 1)
                        nc.scalar.activation(c_sb[:, o], rc_ps[p][o][:, P + B * s:P + B * s + B],
                                             ACT.Tanh).then_inc(s_c[o], 1)

            iterations(act, body)

        @block.vector
        def _(dve):
            nc.vector.memset(ones_sb[:], 1.0).then_inc(s_ones, 1)
            nc.vector.memset(b_parts[:], 0.0).then_inc(s_zero, 1)
            dve.wait_ge(s_b, 2 * DMA)
            nc.vector.tensor_copy(halves_sb[:], halves_raw[:]).then_inc(s_bias, 1)
            dve.wait_ge(s_zero, 1)
            rest = b_raw[:]
            for q in range(PARTS):
                nc.vector.tensor_copy(b_low[:, q], rest).then_inc(s_split, 1)
                nc.vector.tensor_copy(b_parts[32 * q:32 * q + BR], rest).then_inc(s_bias, 1)
                if q < PARTS - 1:
                    dve.wait_ge(s_split, 2 * q + 1)
                    nc.vector.tensor_tensor(b_rest[:, q], rest, b_low[:, q],
                                            ALU.subtract).then_inc(s_split, 1)
                    dve.wait_ge(s_split, 2 * q + 2)
                    rest = b_rest[:, q]

            dve.wait_ge(s_init, DMA)
            dve.wait_ge(s_bq, DMA)

            def body(i, first, last):
                for u in range(US):
                    t = i * US + u
                    p, s = divmod(u, GS)
                    g = i * UG + p
                    old = h_sb[:, :, (u - 1) % US]
                    new = h_sb[:, :, u]
                    for k in range(K):
                        dve.wait_ge(s_r[k], t + 1)
                        nc.vector.tensor_tensor(rh_sb[:, k], r_sb[:, k], old[:, k],
                                                ALU.mult).then_inc(s_rh[k], 1)
                    dve.wait_ge(s_z, t + 1)
                    nc.vector.tensor_tensor(zh_sb[:], z_sb[:], old, ALU.mult)
                    for k in range(K):
                        dve.wait_ge(s_c[k], t + 1)
                        nc.vector.scalar_tensor_tensor(u_sb[:, k], z_sb[:, k], 1.0, c_sb[:, k],
                                                       ALU.subtract, ALU.mult,
                                                       reverse0=True).then_inc(s_u[k], 1)
                    for k in range(K):
                        dve.wait_ge(s_u[k], t + 1)
                        nc.vector.tensor_tensor(new[:, k], zh_sb[:, k], u_sb[:, k],
                                                ALU.add).then_inc(s_h[k], 1)
                    if s == GS - 2 and not (first and p == 0):
                        dve.wait_ge(s_rows[1 - p], DMA * (2 * (i - 1 + p) + 1))
                        nc.vector.tensor_tensor(xrow_sb[:, 1 - p], xrow_sb[:, 1 - p], bq_sb[:],
                                                ALU.add).then_inc(s_xb, 1)
                    if s == GS - 1 and not (first and p == 0):
                        dve.wait_ge(s_xb, g)
                        dve.wait_ge(s_y_ps, g)
                        nc.vector.tensor_tensor(orow_sb[:, 1 - p], y_ps[:, 0:C],
                                                xrow_sb[:, 1 - p], ALU.add).then_inc(s_y, 1)

            iterations(dve, body)
            dve.wait_ge(s_rows[1], DMA * (2 * NIT - 1))
            nc.vector.tensor_tensor(xrow_sb[:, 1], xrow_sb[:, 1], bq_sb[:], ALU.add).then_inc(s_xb, 1)
            dve.wait_ge(s_xb, NG)
            dve.wait_ge(s_y_ps, NG)
            nc.vector.tensor_tensor(orow_sb[:, 1], y_ps[:, 0:C], xrow_sb[:, 1], ALU.add).then_inc(s_y, 1)

        @block.tensor
        def _(pe):
            def mm(ps, weights, moving, start=False, **kw):
                return nc.tensor.matmul(ps, weights, moving, start=start, stop=False,
                                        skip_group_check=True, **kw)

            def state_part(ps, col, w, k, o, moving):
                for j in range(NQ):
                    q = slice(B * j, B * j + B)
                    last = mm(ps[q, col:col + B], w[:, k, P * o + B * j:P * o + B * j + B], moving[:, k],
                              tile_position=(0, B * j))
                return last

            def x_part(p, piece):
                bank, rest = divmod(piece, 2 * K)
                half, k = divmod(rest, K)
                ps = z_ps[p] if bank == K else rc_ps[p][bank]
                gate, o = (Z, half) if bank == K else ((R, N)[half], bank)
                if rest == 0:
                    mm(ps[:, 0:2 * P], b_parts[:, bank], halves_sb[:].rearrange("p h c -> p (h c)"),
                       start=True)
                last = mm(ps[:, P * half:P * half + P], wx_sb[:, gate, k, P * o:P * o + P], xt_sb[:, p, k])
                if piece == 6 * K - 1:
                    last.then_inc(s_xt_used, 1)

            def output_part(p, piece):
                half, k = divmod(piece, K)
                n = slice(P * half, P * half + P)
                last = mm(y_ps[:, n], h_sb[:, k, GS * p:GS * p + GS], whq_sb[:, k, n], start=piece == 0)
                if piece == 2 * K - 1:
                    last.then_inc(s_y_ps, 1)

            pe.wait_ge(s_ones, 1)
            for _ in range(WARM):
                mm(y_ps[:, 0:P], ones_sb[:], ones_sb[:], start=True)
            pe.wait_ge(s_bias, 1 + PARTS)
            pe.wait_ge(s_xt[0], DMA)
            pe.wait_ge(s_wx, 3 * DMA)
            for piece in range(6 * K):
                x_part(0, piece)
            pe.wait_ge(s_init, DMA)
            pe.wait_ge(s_wh, 4 * DMA)

            def body(i, first, last):
                for u in range(US):
                    t = i * US + u
                    p, s = divmod(u, GS)
                    g = i * UG + p
                    old = h_sb[:, :, (u - 1) % US]
                    for o in range(K):
                        for k in range(K):
                            if o == 0 and not (first and u == 0):
                                pe.wait_ge(s_h[k], t)
                            r_mm = state_part(rc_ps[p][o], B * s, whr_sb, k, o, old)
                        r_mm.then_inc(s_r_ps[o], 1)
                    for o in range(K):
                        for k in range(K):
                            z_mm = state_part(z_ps[p], P * o + B * s, whz_sb, k, o, old)
                    z_mm.then_inc(s_z_ps, 1)
                    for k in range(K):
                        pe.wait_ge(s_rh[k], t + 1)
                        for o in range(K):
                            if k == 0 and o == 1:
                                pe.wait_ge(s_r[1], t + 1)
                            c_mm = state_part(rc_ps[p][o], P + B * s, whh_sb, k, o, rh_sb)
                            if k == K - 1:
                                c_mm.then_inc(s_c_ps[o], 1)
                    if not (last and p == 1):
                        if s == 0:
                            pe.wait_ge(s_xt[1 - p], DMA * (i + 1 + p))
                        for piece in range(3 * s, 3 * s + 3):
                            x_part(1 - p, piece)
                    if not (first and p == 0):
                        if s == 0 and not (first and p == 1):
                            pe.wait_ge(s_y, g - 1)
                        output_part(1 - p, s)

            iterations(pe, body)
            pe.wait_ge(s_y, NG - 1)
            for k in range(K):
                pe.wait_ge(s_h[k], T)
            for piece in range(2 * K):
                output_part(1, piece)


def kernel(x, cond_1024, L0_cond_Wxz, L0_cond_bxz, L0_cond_Whz, L0_cond_bhz, L0_cond_Wxr, L0_cond_bxr,
           L0_cond_Whr, L0_cond_bhr, L0_cond_Wxh, L0_cond_bxh, L0_cond_Whh, L0_cond_bhh, L0_cond_Whq,
           L0_cond_bhq):
    import numpy as np
    import concourse.bacc as bacc
    from concourse.bass_utils import run_bass_kernel_spmd

    def contraction_first(w):
        return np.asarray(w).T.reshape(K, P, C).transpose(1, 0, 2)

    x = np.asarray(x)
    bx = {Z: L0_cond_bxz, R: L0_cond_bxr, N: L0_cond_bxh}
    bh = {Z: L0_cond_bhz, R: L0_cond_bhr, N: L0_cond_bhh}

    def bias_rows(gate, o):
        return [np.asarray(b[gate]).reshape(K, P)[o] for b in (bx, bh)]

    bias = np.stack([np.stack(bias_rows(R, o) + bias_rows(N, o)) for o in range(K)]
                    + [np.stack(bias_rows(Z, 0) + bias_rows(Z, 1))], axis=1)
    halves = np.zeros((BK, 2, P), np.float32)
    for q in range(PARTS):
        for half in range(2):
            halves[32 * q + 2 * half:32 * q + 2 * half + 2, half] = 1.0
    arrays = {
        "xt": x.transpose(2, 1, 0).reshape(K, P, NG, P).transpose(2, 1, 0, 3),
        "xrows": x.reshape(B, NG, GS, C).transpose(1, 2, 0, 3).reshape(NG, P, C),
        "h0t": np.asarray(cond_1024).T.reshape(K, P, B).transpose(1, 0, 2),
        "wx": np.stack([contraction_first(w) for w in (L0_cond_Wxz, L0_cond_Wxr, L0_cond_Wxh)]),
        "whz": contraction_first(L0_cond_Whz),
        "whr": contraction_first(L0_cond_Whr),
        "whh": contraction_first(L0_cond_Whh),
        "whq": contraction_first(L0_cond_Whq),
        "bias": bias,
        "bq": np.broadcast_to(np.asarray(L0_cond_bhq), (P, C)),
        "halves": halves,
    }
    nc = bacc.Bacc("TRN2", target_bir_lowering=False, num_devices=1)
    args, feed = [], {}
    for name, a in arrays.items():
        a = np.ascontiguousarray(a)
        feed[f"in_{name}_dram"] = a
        args.append(nc.dram_tensor(f"in_{name}_dram", a.shape, mybir.dt.from_np(a.dtype),
                                   kind="ExternalInput").ap())
    args.append(nc.dram_tensor("out_dram", (NG, P, C), mybir.dt.float32, kind="ExternalOutput").ap())
    gru_kernel(nc, *args)
    r = run_bass_kernel_spmd(nc, [feed], core_ids=[0])
    rows = r.results[0]["out_dram"]
    return rows.reshape(NG, GS, B, C).transpose(2, 0, 1, 3).reshape(B, T, C)
```

```python
import concourse.bass as bass
from concourse import mybir
from contextlib import ExitStack

B = 32
T = 256
C = 256
P = 128
K = C // P
NQ = P // B
GS = P // B
NG = T // GS
UG = 2
US = UG * GS
NIT = NG // UG
DMA = 16
Z, R, N = range(3)
FIRST_USE = {0: R, K: N, 4 * K: Z}
WARM = 60


def gru_kernel(nc, xt, xrows, h0t, wx, whz, whr, whh, whq, bx, bh, bq, out):
    fp32 = mybir.dt.float32
    bf16 = mybir.dt.bfloat16
    ALU = mybir.AluOpType
    ACT = mybir.ActivationFunctionType

    ctx = ExitStack()
    with ctx:
        def sb(name, shape, dt=fp32):
            return ctx.enter_context(nc.sbuf_tensor(name, shape, dt))

        def pb(name):
            return ctx.enter_context(nc.psum_tensor(name, [P, 2 * P * K], fp32))

        def sem(name):
            return ctx.enter_context(nc.semaphore(name))

        wx_sb = sb("wx_sb", [P, 3, K, C])
        whz_sb = sb("whz_sb", [P, K, C])
        whr_sb = sb("whr_sb", [P, K, C])
        whh_sb = sb("whh_sb", [P, K, C])
        whq_sb = sb("whq_sb", [P, K, C])
        bx_sb = sb("bx_sb", [P, 3, K])
        bh_sb = sb("bh_sb", [P, 3, K])
        b_sb = sb("b_sb", [P, 3, K])
        bq_sb = sb("bq_sb", [P, C])
        ones_sb = sb("ones_sb", [P, P], bf16)
        act_warm = sb("act_warm", [1, 1])
        xt_sb = sb("xt_sb", [P, UG, K, P])
        xrow_sb = sb("xrow_sb", [P, UG, C])
        orow_sb = sb("orow_sb", [P, UG, C])
        h_sb = sb("h_sb", [P, K, US, B])
        r_sb = sb("r_sb", [P, K, B])
        rh_sb = sb("rh_sb", [P, K, B])
        z_sb = sb("z_sb", [P, K, B])
        zh_sb = sb("zh_sb", [P, K, B])
        c_sb = sb("c_sb", [P, K, B])
        u_sb = sb("u_sb", [P, K, B])

        rc_ps = [[pb(f"rc_ps{p}{o}") for o in range(K)] for p in range(UG)]
        z_ps = [pb(f"z_ps{p}") for p in range(UG)]
        y_ps = pb("y_ps")

        s_wx = [sem(f"s_wx{gate}") for gate in (Z, R, N)]
        s_whz = sem("s_whz")
        s_whr = sem("s_whr")
        s_whh = sem("s_whh")
        s_whq = sem("s_whq")
        s_b = sem("s_b")
        s_bq = sem("s_bq")
        s_init = sem("s_init")
        s_xt = [sem(f"s_xt{p}") for p in range(UG)]
        s_rows = [sem(f"s_rows{p}") for p in range(UG)]
        s_ones = sem("s_ones")
        s_bias = sem("s_bias")
        s_xt_used = sem("s_xt_used")
        s_r_ps = [sem(f"s_r_ps{o}") for o in range(K)]
        s_z_ps = sem("s_z_ps")
        s_c_ps = [sem(f"s_c_ps{o}") for o in range(K)]
        s_y_ps = sem("s_y_ps")
        s_r = [sem(f"s_r{o}") for o in range(K)]
        s_z = [sem(f"s_z{o}") for o in range(K)]
        s_c = [sem(f"s_c{o}") for o in range(K)]
        s_rh = [sem(f"s_rh{k}") for k in range(K)]
        s_u = [sem(f"s_u{k}") for k in range(K)]
        s_h = [sem(f"s_h{k}") for k in range(K)]
        s_xb = sem("s_xb")
        s_y = sem("s_y")

        block = ctx.enter_context(nc.Block())

        def iterations(eng, body):
            body(0, True, False)
            with eng.Fori(1, NIT - 1) as i:
                body(i, False, False)
            body(NIT - 1, False, True)

        @block.sync
        def _(sp):
            sp.dma_start(xt_sb[:, 0], xt[0]).then_inc(s_xt[0], DMA)
            sp.dma_start(wx_sb[:, R], wx[R]).then_inc(s_wx[R], DMA)
            sp.dma_start(wx_sb[:, Z], wx[Z]).then_inc(s_wx[Z], DMA)
            sp.dma_start(whz_sb[:], whz).then_inc(s_whz, DMA)
            sp.dma_start(xt_sb[:, 1], xt[1]).then_inc(s_xt[1], DMA)
            sp.dma_start(whq_sb[:], whq).then_inc(s_whq, DMA)
            for p in range(UG):
                sp.dma_start(xrow_sb[:, p], xrows[p]).then_inc(s_rows[p], DMA)

            def body(i, first, last):
                for p in range(UG):
                    g = i * UG + p
                    if not last:
                        sp.wait_ge(s_xt_used, g + 1)
                        sp.dma_start(xt_sb[:, p], xt[g + 2]).then_inc(s_xt[p], DMA)
                    if not (first and p == 0):
                        sp.wait_ge(s_y, g)
                        sp.dma_start(out[g - 1], orow_sb[:, 1 - p]).then_inc(s_rows[1 - p], DMA)
                        if not (last and p == 1):
                            sp.dma_start(xrow_sb[:, 1 - p], xrows[g + 1]).then_inc(s_rows[1 - p], DMA)

            iterations(sp, body)
            sp.wait_ge(s_y, NG)
            sp.dma_start(out[NG - 1], orow_sb[:, 1]).then_inc(s_rows[1], DMA)
            for p in range(UG):
                sp.wait_ge(s_rows[p], DMA * 2 * NIT)

        @block.scalar
        def _(act):
            act.dma_start(wx_sb[:, N], wx[N]).then_inc(s_wx[N], DMA)
            act.dma_start(bx_sb[:], bx).then_inc(s_b, DMA)
            act.dma_start(bh_sb[:], bh).then_inc(s_b, DMA)
            act.dma_start(h_sb[:, :, US - 1], h0t).then_inc(s_init, DMA)
            act.dma_start(whr_sb[:], whr).then_inc(s_whr, DMA)
            act.dma_start(whh_sb[:], whh).then_inc(s_whh, DMA)
            act.dma_start(bq_sb[:], bq).then_inc(s_bq, DMA)
            act.wait_ge(s_ones, 1)
            nc.scalar.activation(act_warm[:], ones_sb[0:1, 0:1], ACT.Sigmoid)
            act.wait_ge(s_bias, 1)

            def body(i, first, last):
                for u in range(US):
                    t = i * US + u
                    p, s = divmod(u, GS)
                    for o in range(K):
                        act.wait_ge(s_r_ps[o], t + 1)
                        nc.scalar.activation(r_sb[:, o], rc_ps[p][o][:, B * s:B * s + B],
                                             ACT.Sigmoid, bias=b_sb[:, R, o:o + 1]).then_inc(s_r[o], 1)
                    act.wait_ge(s_z_ps, t + 1)
                    for o in range(K):
                        nc.scalar.activation(z_sb[:, o], z_ps[p][:, P * o + B * s:P * o + B * s + B],
                                             ACT.Sigmoid, bias=b_sb[:, Z, o:o + 1]).then_inc(s_z[o], 1)
                    for o in range(K):
                        act.wait_ge(s_c_ps[o], t + 1)
                        nc.scalar.activation(c_sb[:, o], rc_ps[p][o][:, P + B * s:P + B * s + B],
                                             ACT.Tanh, bias=b_sb[:, N, o:o + 1]).then_inc(s_c[o], 1)

            iterations(act, body)

        @block.vector
        def _(dve):
            nc.vector.memset(ones_sb[:], 1.0).then_inc(s_ones, 1)
            dve.wait_ge(s_b, 2 * DMA)
            nc.vector.tensor_tensor(b_sb[:], bx_sb[:], bh_sb[:], ALU.add).then_inc(s_bias, 1)
            dve.wait_ge(s_init, DMA)
            dve.wait_ge(s_bq, DMA)

            def body(i, first, last):
                for u in range(US):
                    t = i * US + u
                    p, s = divmod(u, GS)
                    g = i * UG + p
                    old = h_sb[:, :, (u - 1) % US]
                    new = h_sb[:, :, u]
                    for k in range(K):
                        dve.wait_ge(s_r[k], t + 1)
                        nc.vector.tensor_tensor(rh_sb[:, k], r_sb[:, k], old[:, k],
                                                ALU.mult).then_inc(s_rh[k], 1)
                    for k in range(K):
                        dve.wait_ge(s_z[k], t + 1)
                        nc.vector.tensor_tensor(zh_sb[:, k], z_sb[:, k], old[:, k], ALU.mult)
                    for k in range(K):
                        dve.wait_ge(s_c[k], t + 1)
                        nc.vector.scalar_tensor_tensor(u_sb[:, k], z_sb[:, k], 1.0, c_sb[:, k],
                                                       ALU.subtract, ALU.mult,
                                                       reverse0=True).then_inc(s_u[k], 1)
                    for k in range(K):
                        dve.wait_ge(s_u[k], t + 1)
                        nc.vector.tensor_tensor(new[:, k], zh_sb[:, k], u_sb[:, k],
                                                ALU.add).then_inc(s_h[k], 1)
                    if s == GS - 2 and not (first and p == 0):
                        dve.wait_ge(s_rows[1 - p], DMA * (2 * (i - 1 + p) + 1))
                        nc.vector.tensor_tensor(xrow_sb[:, 1 - p], xrow_sb[:, 1 - p], bq_sb[:],
                                                ALU.add).then_inc(s_xb, 1)
                    if s == GS - 1 and not (first and p == 0):
                        dve.wait_ge(s_xb, g)
                        dve.wait_ge(s_y_ps, g)
                        nc.vector.tensor_tensor(orow_sb[:, 1 - p], y_ps[:, 0:C],
                                                xrow_sb[:, 1 - p], ALU.add).then_inc(s_y, 1)

            iterations(dve, body)
            dve.wait_ge(s_rows[1], DMA * (2 * NIT - 1))
            nc.vector.tensor_tensor(xrow_sb[:, 1], xrow_sb[:, 1], bq_sb[:], ALU.add).then_inc(s_xb, 1)
            dve.wait_ge(s_xb, NG)
            dve.wait_ge(s_y_ps, NG)
            nc.vector.tensor_tensor(orow_sb[:, 1], y_ps[:, 0:C], xrow_sb[:, 1], ALU.add).then_inc(s_y, 1)

        @block.tensor
        def _(pe):
            def mm(ps, weights, moving, start=False, **kw):
                return nc.tensor.matmul(ps, weights, moving, start=start, stop=False,
                                        skip_group_check=True, **kw)

            def state_part(ps, col, w, k, o, moving):
                for j in range(NQ):
                    q = slice(B * j, B * j + B)
                    last = mm(ps[q, col:col + B], w[:, k, P * o + B * j:P * o + B * j + B], moving[:, k],
                              tile_position=(0, B * j))
                return last

            def x_part(p, piece):
                bank, rest = divmod(piece, 2 * K)
                half, k = divmod(rest, K)
                ps = z_ps[p] if bank == K else rc_ps[p][bank]
                gate, o = (Z, half) if bank == K else ((R, N)[half], bank)
                last = mm(ps[:, P * half:P * half + P], wx_sb[:, gate, k, P * o:P * o + P], xt_sb[:, p, k],
                          start=rest == 0)
                if piece == 6 * K - 1:
                    last.then_inc(s_xt_used, 1)

            def output_part(p, piece):
                half, k = divmod(piece, K)
                n = slice(P * half, P * half + P)
                last = mm(y_ps[:, n], h_sb[:, k, GS * p:GS * p + GS], whq_sb[:, k, n], start=piece == 0)
                if piece == 2 * K - 1:
                    last.then_inc(s_y_ps, 1)

            pe.wait_ge(s_ones, 1)
            for _ in range(WARM):
                mm(y_ps[:, 0:P], ones_sb[:], ones_sb[:], start=True)
            pe.wait_ge(s_xt[0], DMA)
            for piece in range(6 * K):
                if piece in FIRST_USE:
                    pe.wait_ge(s_wx[FIRST_USE[piece]], DMA)
                x_part(0, piece)
            pe.wait_ge(s_init, DMA)
            pe.wait_ge(s_whr, DMA)

            def body(i, first, last):
                for u in range(US):
                    t = i * US + u
                    p, s = divmod(u, GS)
                    g = i * UG + p
                    old = h_sb[:, :, (u - 1) % US]
                    for o in range(K):
                        for k in range(K):
                            if o == 0 and not (first and u == 0):
                                pe.wait_ge(s_h[k], t)
                            r_mm = state_part(rc_ps[p][o], B * s, whr_sb, k, o, old)
                        r_mm.then_inc(s_r_ps[o], 1)
                    if first and u == 0:
                        pe.wait_ge(s_whz, DMA)
                    for o in range(K):
                        for k in range(K):
                            z_mm = state_part(z_ps[p], P * o + B * s, whz_sb, k, o, old)
                    z_mm.then_inc(s_z_ps, 1)
                    if first and u == 0:
                        pe.wait_ge(s_whh, DMA)
                    for k in range(K):
                        pe.wait_ge(s_rh[k], t + 1)
                        for o in range(K):
                            if k == 0 and o == 1:
                                pe.wait_ge(s_r[1], t + 1)
                            c_mm = state_part(rc_ps[p][o], P + B * s, whh_sb, k, o, rh_sb)
                            if k == K - 1:
                                c_mm.then_inc(s_c_ps[o], 1)
                    if not (last and p == 1):
                        if s == 0:
                            pe.wait_ge(s_xt[1 - p], DMA * (i + 1 + p))
                        for piece in range(3 * s, 3 * s + 3):
                            x_part(1 - p, piece)
                    if not (first and p == 0):
                        if first and s == 0:
                            pe.wait_ge(s_whq, DMA)
                        elif s == 0:
                            pe.wait_ge(s_y, g - 1)
                        output_part(1 - p, s)

            iterations(pe, body)
            pe.wait_ge(s_y, NG - 1)
            for k in range(K):
                pe.wait_ge(s_h[k], T)
            for piece in range(2 * K):
                output_part(1, piece)


def kernel(x, cond_1024, L0_cond_Wxz, L0_cond_bxz, L0_cond_Whz, L0_cond_bhz, L0_cond_Wxr, L0_cond_bxr,
           L0_cond_Whr, L0_cond_bhr, L0_cond_Wxh, L0_cond_bxh, L0_cond_Whh, L0_cond_bhh, L0_cond_Whq,
           L0_cond_bhq):
    import numpy as np
    import concourse.bacc as bacc
    from concourse.bass_utils import run_bass_kernel_spmd

    def contraction_first(w):
        return np.asarray(w).T.reshape(K, P, C).transpose(1, 0, 2)

    x = np.asarray(x)

    def gate_biases(*b):
        return np.stack([np.asarray(v) for v in b]).reshape(3, K, P).transpose(2, 0, 1)

    arrays = {
        "xt": x.transpose(2, 1, 0).reshape(K, P, NG, P).transpose(2, 1, 0, 3),
        "xrows": x.reshape(B, NG, GS, C).transpose(1, 2, 0, 3).reshape(NG, P, C),
        "h0t": np.asarray(cond_1024).T.reshape(K, P, B).transpose(1, 0, 2),
        "wx": np.stack([contraction_first(w) for w in (L0_cond_Wxz, L0_cond_Wxr, L0_cond_Wxh)]),
        "whz": contraction_first(L0_cond_Whz),
        "whr": contraction_first(L0_cond_Whr),
        "whh": contraction_first(L0_cond_Whh),
        "whq": contraction_first(L0_cond_Whq),
        "bx": gate_biases(L0_cond_bxz, L0_cond_bxr, L0_cond_bxh),
        "bh": gate_biases(L0_cond_bhz, L0_cond_bhr, L0_cond_bhh),
        "bq": np.broadcast_to(np.asarray(L0_cond_bhq), (P, C)),
    }
    nc = bacc.Bacc("TRN2", target_bir_lowering=False, num_devices=1)
    args, feed = [], {}
    for name, a in arrays.items():
        a = np.ascontiguousarray(a)
        feed[f"in_{name}_dram"] = a
        args.append(nc.dram_tensor(f"in_{name}_dram", a.shape, mybir.dt.from_np(a.dtype),
                                   kind="ExternalInput").ap())
    args.append(nc.dram_tensor("out_dram", (NG, P, C), mybir.dt.float32, kind="ExternalOutput").ap())
    gru_kernel(nc, *args)
    r = run_bass_kernel_spmd(nc, [feed], core_ids=[0])
    rows = r.results[0]["out_dram"]
    return rows.reshape(NG, GS, B, C).transpose(2, 0, 1, 3).reshape(B, T, C)
```
